# Optimizing a Trainium2 kernel written in Bass

```python
import numpy as np
import jax
import jax.numpy as jnp

def _softmax(x, axis=-1):
    return jax.nn.softmax(x, axis=axis)

def _gelu(x):
    return jax.nn.gelu(x, approximate=True)

def _silu(x):
    return jax.nn.silu(x)

def _sigmoid(x):
    return jax.nn.sigmoid(x)

def _layernorm(x, axis=-1, eps=1e-05):
    m = jnp.mean(x, axis=axis, keepdims=True)
    v = jnp.var(x, axis=axis, keepdims=True)
    return (x - m) / jnp.sqrt(v + eps)

def _scatter_add(tgt, idx, src, axis=0):
    return tgt.at[idx].add(src)

def _segment_sum(src, seg, n):
    return jax.ops.segment_sum(src, seg, n)
kernel_name = 'mk_adaln_ffn_d1_seqx_r4_022e07'

def setup_inputs(seed: int=0):
    np.random.seed(seed)
    _w = jnp.asarray

    def _rec_inputs():
        import jax
        import jax.numpy as jnp
        _rk = jax.random.key(seed)
        x = -8.015e-05 + 0.9999 * jax.random.normal(jax.random.fold_in(_rk, 1), (16, 256, 512), jnp.float32)
        _lenS = 256 - jax.random.randint(jax.random.fold_in(_rk, 7), (16,), 0, max(1, 256 // 4) + 1, jnp.int32)
        _lenS2 = 256 - jax.random.randint(jax.random.fold_in(_rk, 8), (16,), 0, max(1, 256 // 4) + 1, jnp.int32)
        cond_1024 = 0.00191187 + 0.999416 * jax.random.normal(jax.random.fold_in(_rk, 11), (16, 256), jnp.float32)
        return (x, cond_1024)
    x, cond_1024 = _rec_inputs()

    def _L0_cond_setup():
        import jax, jax.numpy as jnp
        import numpy as np
        B, N, V_DIM, Q_DIM = (64, 100, 512, 256)
        key = jax.random.key(seed)
        k1, k2, k3, k4 = jax.random.split(key, 4)
        v = jax.random.normal(k1, (B, N, V_DIM), dtype=jnp.float32)
        q = jax.random.normal(k2, (B, Q_DIM), dtype=jnp.float32)
        W3 = jax.random.normal(k3, (Q_DIM, V_DIM), dtype=jnp.float32) * (1.0 / np.sqrt(Q_DIM))
        b3 = jnp.zeros((V_DIM,), dtype=jnp.float32)
        W2 = jax.random.normal(k4, (V_DIM, V_DIM), dtype=jnp.float32) * (1.0 / np.sqrt(V_DIM))
        b2 = jnp.zeros((V_DIM,), dtype=jnp.float32)
        return {'v': v, 'q': q, 'W3': W3, 'b3': b3, 'W2': W2, 'b2': b2}
    _L0_cond_all = _L0_cond_setup()
    _L0_cond_in = {k: v for k, v in _L0_cond_all.items() if k in ('W3', 'b3', 'W2', 'b2')}
    del _L0_cond_all

    def _L0_ffn_setup():
        import jax, jax.numpy as jnp
        import numpy as np

        def ternary_quantize(t, threshold, scale):
            return jnp.where(t > threshold, scale, jnp.where(t < -threshold, -scale, 0.0)).astype(t.dtype)
        key = jax.random.key(seed)
        k1, k2, k3 = jax.random.split(key, 3)
        B, S, D = (4, 1024, 512)
        x = jax.random.normal(k1, (B, S, D), dtype=jnp.float32)
        weight = jax.random.normal(k2, (D, D), dtype=jnp.float32) * 0.02
        rram_variation = jax.random.normal(k3, (D, D), dtype=jnp.float32) * 0.05
        return {'x': x, 'weight': weight, 'rram_variation': rram_variation}
    _L0_ffn_all = _L0_ffn_setup()
    _L0_ffn_in = {k: v for k, v in _L0_ffn_all.items() if k in ('weight', 'rram_variation')}
    del _L0_ffn_all
    return {'x': x, 'cond_1024': cond_1024, 'L0_cond_W3': _L0_cond_in['W3'], 'L0_cond_b3': _L0_cond_in['b3'], 'L0_cond_W2': _L0_cond_in['W2'], 'L0_cond_b2': _L0_cond_in['b2'], 'L0_ffn_weight': _L0_ffn_in['weight'], 'L0_ffn_rram_variation': _L0_ffn_in['rram_variation']}

def reference(x, cond_1024, L0_cond_W3, L0_cond_b3, L0_cond_W2, L0_cond_b2, L0_ffn_weight, L0_ffn_rram_variation):
    import jax
    import jax.numpy as jnp

    def _L0_cond_ref(v, q, W3, b3, W2, b2):
        import jax, jax.numpy as jnp
        import numpy as np
        B, N, V_DIM, Q_DIM = (64, 100, 512, 256)
        q_emb = jax.nn.relu(q @ W3 + b3)
        n = v.shape[1]
        v_sum = jnp.sum(v, axis=1, keepdims=True)
        x = (n * v + v_sum) * q_emb[:, None, :]
        return jax.nn.relu(x @ W2 + b2)

    def _L0_ffn_ref(x, weight, rram_variation):
        import jax, jax.numpy as jnp
        import numpy as np

        def ternary_quantize(t, threshold, scale):
            return jnp.where(t > threshold, scale, jnp.where(t < -threshold, -scale, 0.0)).astype(t.dtype)
        TH_X, SC_X = (0.33, 0.5)
        TH_W, SC_W = (0.2, 0.6)
        x_q = ternary_quantize(x, TH_X, SC_X)
        w_q = ternary_quantize(weight, TH_W, SC_W)
        w_rram = w_q + rram_variation
        return jnp.einsum('bsd,od->bso', x_q, w_rram)
    x = x + _L0_ffn_ref(_L0_cond_ref(x, cond_1024, L0_cond_W3, L0_cond_b3, L0_cond_W2, L0_cond_b2), L0_ffn_weight, L0_ffn_rram_variation)
    return x

_drawn_inputs = setup_inputs


def setup_inputs(seed=0):
    import zlib

    import numpy as np

    out = dict(_drawn_inputs(seed))
    spreads = {'L0_cond_b3': (0.0, 0.1), 'L0_cond_b2': (0.0, 2.0)}
    factors = {}
    for name, (base, spread) in spreads.items():
        noise = np.random.default_rng([zlib.crc32(name.encode()), seed]).standard_normal(out[name].shape)
        drawn = base * np.exp(spread * noise) if base else spread * noise
        out[name] = jnp.asarray(drawn.astype(out[name].dtype))
    for name, factor in factors.items():
        out[name] = (out[name] * factor).astype(out[name].dtype)
    return out
```

```python
import concourse.bass as bass
from concourse import mybir
from contextlib import ExitStack


def adaln_ffn_kernel(
    nc: bass.Bass,
    x: bass.AP,
    cond: bass.AP,
    w3: bass.AP,
    b3: bass.AP,
    w2: bass.AP,
    b2: bass.AP,
    weight: bass.AP,
    rram: bass.AP,
    out: bass.AP,
):
    F32 = mybir.dt.float32
    F32R = mybir.dt.float32r
    ALU = mybir.AluOpType
    ACT = mybir.ActivationFunctionType
    AX = mybir.AxisListType

    B, N, D = x.shape
    C = cond.shape[1]
    P = 128
    BLK = 32
    QUADS = P // BLK
    KD = D // P
    KC = C // P
    GB = 2
    GT = GB * N
    GROUPS = B // GB
    TILES = GT // P
    NB = N // BLK
    FQ = D // QUADS
    CQ = C // QUADS
    OB = D // BLK
    DMA = 16
    TH_X, SC_X = 0.33, 0.5
    TH_W, SC_W = 0.2, 0.6

    x_rows = x.rearrange("b n d -> (b n) d")
    out_rows = out.rearrange("b n d -> (b n) d")
    x_split = x_rows.rearrange("(g n t) (q f) -> g q t n f", n=GB * NB, t=BLK, q=QUADS)
    x_tiles = x_rows.rearrange("(g c p) d -> g p c d", c=TILES, p=P)
    out_tiles = out_rows.rearrange("(g c p) d -> g c p d", c=TILES, p=P)
    cond_split = cond.rearrange("b (q f) -> q b f", q=QUADS)
    w2_chunks = w2.rearrange("(p j) n -> p j n", j=KD)
    w3_chunks = w3.rearrange("(p j) n -> p j n", j=KC)
    b2_chunks = b2.rearrange("(p j) -> p j", j=KD)
    b3_chunks = b3.rearrange("(p j) -> p j", j=KD)
    weight_split = weight.rearrange("(n t) (q f) -> q t n f", t=BLK, q=QUADS)
    rram_split = rram.rearrange("(n t) (q f) -> q t n f", t=BLK, q=QUADS)

    ctx = ExitStack()
    with ctx:
        def sbuf(name, shape, dt=F32):
            return ctx.enter_context(nc.sbuf_tensor(name, shape, dt))

        def psum(name, shape):
            return ctx.enter_context(nc.psum_tensor(name, shape, F32))

        def sem(name):
            return ctx.enter_context(nc.semaphore(name))

        x_in = sbuf("x_in", [P, 2, GB * NB, FQ])
        x_res = sbuf("x_res", [P, 2, TILES, D])
        xT = sbuf("xT", [P, 2, KD, GT])
        hid = sbuf("hid", [P, 2, KD, GT], F32R)
        x_sum = sbuf("x_sum", [P, GB, KD])
        coef = sbuf("coef", [P, 2, GB, KD])
        q_scale = sbuf("q_scale", [P, B, KD])
        q_emb = sbuf("q_emb", [P, B, KD])
        cond_in = sbuf("cond_in", [P, CQ])
        condT = sbuf("condT", [P, KC, BLK])
        b2_col = sbuf("b2_col", [P, KD])
        b3_col = sbuf("b3_col", [P, KD])
        w2_sb = sbuf("w2_sb", [P, KD, D])
        w3_sb = sbuf("w3_sb", [P, KC, D])
        w_in = sbuf("w_in", [P, OB, FQ])
        r_in = sbuf("r_in", [P, OB, FQ])
        w_low = sbuf("w_low", [P, OB, FQ])
        wT = sbuf("wT", [P, KD, D])
        wT_hi = sbuf("wT_hi", [P, KD, D], F32R)
        wT_lo = sbuf("wT_lo", [P, KD, D], F32R)

        hid_ps = [psum(f"hid_ps{m}", [P, GT]) for m in range(KD)]
        out_ps = [psum(f"out_ps{c}", [P, D]) for c in range(TILES)]
        q_ps = out_ps[0]

        def chunk_columns(w, m):
            return w.rearrange("p (c m) -> p m c", m=KD)[:, m]

        s_x_in = [sem(f"x_in_loaded{s}") for s in range(2)]
        s_x_res = [sem(f"x_res_loaded{s}") for s in range(2)]
        s_stored = [sem(f"stored{s}") for s in range(2)]
        s_x_first = sem("first_batch_loaded")
        s_cond_zero = sem("cond_zeroed")
        s_cond = sem("cond_loaded")
        s_b2 = sem("b2_loaded")
        s_b3 = sem("b3_loaded")
        s_w3 = sem("w3_loaded")
        s_w2 = [sem(f"w2_loaded{k}") for k in range(KD)]
        s_w = sem("weight_loaded")
        s_r = sem("rram_loaded")
        s_condT = sem("cond_transposed")
        s_q_ps = sem("q_product_ready")
        s_q = sem("q_ready")
        s_xT = sem("x_transposed")
        s_sum = sem("x_summed")
        s_coef = sem("coef_ready")
        s_xs = sem("x_scaled")
        s_hid_ps = sem("hidden_product_ready")
        s_hid = sem("hidden_ready")
        s_out_ps = sem("out_product_ready")
        s_out = sem("out_tile_ready")
        s_wpool = sem("weight_step_done")
        s_wT = sem("weight_transposed")
        s_whi = sem("weight_hi_ready")
        s_wlo = sem("weight_lo_ready")

        block = ctx.enter_context(nc.Block())

        @block.sync
        def _(sp):
            def load_x_in(t, s):
                for q in (0, 2, 1, 3):
                    sp.dma_start(x_in[q * BLK:(q + 1) * BLK, s], x_split[2 * t + s, q]).then_inc(s_x_in[s], DMA)

            def load_x_res(t, s):
                sp.dma_start(x_res[:, s], x_tiles[2 * t + s]).then_inc(s_x_res[s], DMA)

            def store(t, s):
                for c in range(TILES):
                    sp.wait_ge(s_out, TILES * (2 * t + s) + c + 1)
                    sp.dma_start(out_tiles[2 * t + s, c], x_res[:, s, c]).then_inc(s_stored[s], DMA)

            def reload_x_in(t, s):
                sp.wait_ge(s_xT, GB * (2 * (t - 1) + s + 1))
                load_x_in(t, s)

            def reload_x_res(t, s):
                sp.wait_ge(s_stored[s], DMA * TILES * t)
                load_x_res(t, s)

            for b in range(GB):
                for q in (0, 2, 1, 3):
                    sp.dma_start(x_in[q * BLK:(q + 1) * BLK, 0, b * NB:(b + 1) * NB],
                                 x_split[0, q, :, b * NB:(b + 1) * NB]).then_inc(s_x_in[0] if b else s_x_first, DMA)
            load_x_in(0, 1)
            for q in range(QUADS):
                sp.dma_start(w_in[q * BLK:(q + 1) * BLK], weight_split[q]).then_inc(s_w, DMA)
            for q in range(QUADS):
                sp.dma_start(r_in[q * BLK:(q + 1) * BLK], rram_split[q]).then_inc(s_r, DMA)
            load_x_res(0, 0)
            reload_x_in(1, 0)
            load_x_res(0, 1)
            with sp.Fori(0, GROUPS // 2 - 2) as t:
                reload_x_in(t + 1, 1)
                store(t, 0)
                reload_x_res(t + 1, 0)
                reload_x_in(t + 2, 0)
                store(t, 1)
                reload_x_res(t + 1, 1)
            last = GROUPS // 2 - 1
            reload_x_in(last, 1)
            store(last - 1, 0)
            reload_x_res(last, 0)
            store(last - 1, 1)
            reload_x_res(last, 1)
            store(last, 0)
            store(last, 1)
            for s in range(2):
                sp.wait_ge(s_stored[s], DMA * TILES * GROUPS // 2)

        @block.gpsimd
        def _(pool):
            nc.gpsimd.memset(cond_in[:], 0.0).then_inc(s_cond_zero, 1)
            pool.wait_ge(s_w, QUADS * DMA)
            nc.gpsimd.tensor_scalar(w_low[:], w_in[:], -TH_W, -SC_W, ALU.is_lt, ALU.mult).then_inc(s_wpool, 1)
            pool.wait_ge(s_wpool, 1)
            nc.gpsimd.tensor_scalar(w_in[:], w_in[:], TH_W, SC_W, ALU.is_gt, ALU.mult).then_inc(s_wpool, 1)
            pool.wait_ge(s_wpool, 2)
            nc.gpsimd.tensor_tensor(w_in[:], w_in[:], w_low[:], ALU.add).then_inc(s_wpool, 1)
            pool.wait_ge(s_r, QUADS * DMA)
            pool.wait_ge(s_wpool, 3)
            nc.gpsimd.tensor_tensor(w_in[:], w_in[:], r_in[:], ALU.add).then_inc(s_wpool, 1)

        @block.scalar
        def _(act):
            act.dma_start(w3_sb[:], w3_chunks).then_inc(s_w3, DMA)
            act.wait_ge(s_cond_zero, 1)
            for q in range(QUADS):
                act.dma_start(cond_in[q * BLK:q * BLK + B], cond_split[q]).then_inc(s_cond, DMA)
            act.dma_start(b3_col[:], b3_chunks).then_inc(s_b3, DMA)
            for k in range(KD):
                act.dma_start(w2_sb[:, k], w2_chunks[:, k]).then_inc(s_w2[k], DMA)
            act.dma_start(b2_col[:], b2_chunks).then_inc(s_b2, DMA)

            act.wait_ge(s_b3, DMA)
            act.wait_ge(s_q_ps, 1)
            for m in range(KD):
                nc.scalar.activation(q_emb[:, :, m], q_ps[:, m * B:(m + 1) * B], ACT.Relu,
                                     bias=b3_col[:, m:m + 1]).then_inc(s_q, 1)
            act.wait_ge(s_q, KD)
            nc.scalar.mul(q_scale[:], q_emb[:], float(N)).then_inc(s_q, 1)
            act.wait_ge(s_q, KD + 1)

            def scale(t, s):
                for b in range(GB):
                    act.wait_ge(s_coef, GB * (2 * t + s) + b + 1)
                    for k in range(KD):
                        part = xT[:, s, k, b * N:(b + 1) * N]
                        nc.scalar.activation(part, part, ACT.Identity, bias=coef[:, s, b, k:k + 1],
                                             scale=q_scale[:, GB * (2 * t + s) + b, k:k + 1]).then_inc(s_xs, 1)

            scale(0, 0)
            scale(0, 1)
            act.wait_ge(s_wT, 1)
            nc.scalar.copy(wT_hi[:], wT[:]).then_inc(s_whi, 1)
            with act.Fori(0, GROUPS // 2 - 1) as t:
                scale(t + 1, 0)
                scale(t + 1, 1)

        @block.vector
        def _(dve):
            def prepare(t, s, recycled, first=False):
                for b in range(GB):
                    n = GB * (2 * t + s) + b
                    rows = slice(b * NB, (b + 1) * NB)
                    if first and b == 0:
                        dve.wait_ge(s_x_first, DMA * QUADS)
                    else:
                        dve.wait_ge(s_x_in[s], DMA * QUADS * (t + 1))
                    if recycled:
                        dve.wait_ge(s_hid_ps, KD * (2 * (t - 1) + s + 1))
                    nc.vector.transpose(
                        xT[:, s, :, b * N:(b + 1) * N].rearrange("p j (n t) -> p n j t", t=BLK),
                        x_in[:, s, rows].rearrange("p n (r j) -> p n j r", r=BLK)).then_inc(s_xT, 1)
                    dve.wait_ge(s_xT, n + 1)
                    nc.vector.tensor_reduce(x_sum[:, b], xT[:, s, :, b * N:(b + 1) * N],
                                            AX.X, ALU.add).then_inc(s_sum, 1)
                    dve.wait_ge(s_sum, n + 1)
                    if not recycled:
                        dve.wait_ge(s_q, KD + 1)
                    nc.vector.tensor_tensor(coef[:, s, b], x_sum[:, b], q_emb[:, n], ALU.mult).then_inc(s_coef, 1)

            def quantize(t, s):
                for m in range(KD):
                    dve.wait_ge(s_hid_ps, KD * (2 * t + s) + m + 1)
                    nc.vector.tensor_scalar(hid[:, s, m], hid_ps[m][:], b2_col[:, m:m + 1], TH_X,
                                            ALU.add, ALU.is_gt).then_inc(s_hid, 1)

            def finish(t, s):
                dve.wait_ge(s_x_res[s], DMA * (t + 1))
                for c in range(TILES):
                    dve.wait_ge(s_out_ps, TILES * (2 * t + s) + c + 1)
                    nc.vector.scalar_tensor_tensor(x_res[:, s, c], out_ps[c][:], SC_X, x_res[:, s, c],
                                                   ALU.mult, ALU.add).then_inc(s_out, 1)

            dve.wait_ge(s_cond, QUADS * DMA)
            nc.vector.transpose(condT[:], cond_in[:].rearrange("p (r j) -> p j r", j=KC)).then_inc(s_condT, 1)
            prepare(0, 0, False, first=True)
            prepare(0, 1, False)
            dve.wait_ge(s_b2, DMA)
            quantize(0, 0)
            dve.wait_ge(s_wpool, 4)
            nc.vector.transpose(wT[:].rearrange("p j (n t) -> p n j t", t=BLK),
                                w_in[:].rearrange("p n (r j) -> p n j r", r=BLK)).then_inc(s_wT, 1)
            dve.wait_ge(s_whi, 1)
            nc.vector.tensor_tensor(wT_lo[:], wT[:], wT_hi[:].bitcast(F32), ALU.subtract).then_inc(s_wlo, 1)
            with dve.Fori(0, GROUPS // 2 - 1) as t:
                prepare(t + 1, 0, True)
                quantize(t, 1)
                finish(t, 0)
                prepare(t + 1, 1, True)
                quantize(t + 1, 0)
                finish(t, 1)
            last = GROUPS // 2 - 1
            quantize(last, 1)
            finish(last, 0)
            finish(last, 1)

        @block.tensor
        def _(pe):
            pe.wait_ge(s_condT, 1)
            pe.wait_ge(s_w3, DMA)
            for m in range(KD):
                for k in range(KC):
                    mm = nc.tensor.matmul(q_ps[:, m * B:(m + 1) * B], chunk_columns(w3_sb[:, k], m),
                                          condT[:, k, 0:B], start=(k == 0), stop=(k == KC - 1))
            mm.then_inc(s_q_ps, 1)

            def hidden(t, s):
                pe.wait_ge(s_xs, GB * KD * (2 * t + s + 1))
                for m in range(KD):
                    pe.wait_ge(s_hid, KD * (2 * t + s - 1) + m + 1)
                    for k in range(KD):
                        mm = nc.tensor.matmul(hid_ps[m][:], chunk_columns(w2_sb[:, k], m), xT[:, s, k],
                                              start=(k == 0), stop=(k == KD - 1))
                    mm.then_inc(s_hid_ps, 1)

            def project(t, s, first):
                pe.wait_ge(s_hid, KD * (2 * t + s + 1))
                for c in range(TILES):
                    if not first:
                        pe.wait_ge(s_out, TILES * (2 * t + s - 1) + c + 1)
                    for k in range(KD):
                        for w in (wT_lo, wT_hi):
                            mm = nc.tensor.matmul(out_ps[c][:], hid[:, s, k, c * P:(c + 1) * P], w[:, k],
                                                  start=(k == 0 and w is wT_lo), stop=(k == KD - 1 and w is wT_hi))
                    mm.then_inc(s_out_ps, 1)

            for k in range(KD):
                pe.wait_ge(s_w2[k], DMA)
                pe.wait_ge(s_xs, k + 1)
                for m in range(KD):
                    nc.tensor.matmul(hid_ps[m][:, 0:N], chunk_columns(w2_sb[:, k], m), xT[:, 0, k, 0:N],
                                     start=(k == 0), stop=(k == KD - 1))
            pe.wait_ge(s_xs, 2 * KD)
            for m in range(KD):
                for k in range(KD):
                    mm = nc.tensor.matmul(hid_ps[m][:, N:GT], chunk_columns(w2_sb[:, k], m), xT[:, 0, k, N:GT],
                                          start=(k == 0), stop=(k == KD - 1))
                mm.then_inc(s_hid_ps, 1)

            hidden(0, 1)
            pe.wait_ge(s_wlo, 1)
            project(0, 0, True)
            with pe.Fori(0, GROUPS // 2 - 1) as t:
                hidden(t + 1, 0)
                project(t, 1, False)
                hidden(t + 1, 1)
                project(t + 1, 0, False)
            project(GROUPS // 2 - 1, 1, False)


_INS = ["x", "cond_1024", "L0_cond_W3", "L0_cond_b3", "L0_cond_W2", "L0_cond_b2", "L0_ffn_weight",
        "L0_ffn_rram_variation"]


def kernel(**inputs):
    import numpy as np
    import concourse.bacc as bacc
    from concourse import mybir as mb
    from concourse.bass_utils import run_bass_kernel_spmd

    nc = bacc.Bacc("TRN2", target_bir_lowering=False, num_devices=1)
    arrays, args = {}, []
    for name in _INS:
        a = np.ascontiguousarray(inputs[name])
        arrays[f"in_{name}"] = a
        args.append(nc.dram_tensor(f"in_{name}", a.shape, mb.dt.from_np(a.dtype), kind="ExternalInput").ap())
    shape = inputs["x"].shape
    args.append(nc.dram_tensor("out", shape, mb.dt.float32, kind="ExternalOutput").ap())
    adaln_ffn_kernel(nc, *args)
    r = run_bass_kernel_spmd(nc, [arrays], core_ids=[0])
    return r.results[0]["out"]
```

```python
import concourse.bass as bass
from concourse import mybir
from contextlib import ExitStack


def adaln_ffn_kernel(
    nc: bass.Bass,
    x: bass.AP,
    cond: bass.AP,
    w3: bass.AP,
    b3: bass.AP,
    w2: bass.AP,
    b2: bass.AP,
    weight: bass.AP,
    rram: bass.AP,
    out: bass.AP,
):
    F32 = mybir.dt.float32
    F32R = mybir.dt.float32r
    ALU = mybir.AluOpType
    ACT = mybir.ActivationFunctionType
    AX = mybir.AxisListType

    B, N, D = x.shape
    C = cond.shape[1]
    P = 128
    BLK = 32
    QUADS = P // BLK
    KD = D // P
    KC = C // P
    GB = 2
    GT = GB * N
    GROUPS = B // GB
    TILES = GT // P
    NB = N // BLK
    FQ = D // QUADS
    CQ = C // QUADS
    OB = D // BLK
    DMA = 16
    WARM, WARM_2 = 8, 13
    TH_X, SC_X = 0.33, 0.5
    TH_W, SC_W = 0.2, 0.6

    x_rows = x.rearrange("b n d -> (b n) d")
    out_rows = out.rearrange("b n d -> (b n) d")
    x_split = x_rows.rearrange("(g n t) (q f) -> g q t n f", n=GB * NB, t=BLK, q=QUADS)
    x_tiles = x_rows.rearrange("(g c p) d -> g p c d", c=TILES, p=P)
    out_tiles = out_rows.rearrange("(g c p) d -> g c p d", c=TILES, p=P)
    w2_chunks = w2.rearrange("(p j) n -> p j n", j=KD)
    w3_chunks = w3.rearrange("(p j) n -> p j n", j=KC)
    b2_chunks = b2.rearrange("(p j) -> p j", j=KD)
    b3_chunks = b3.rearrange("(p j) -> p j", j=KD)
    weight_split = weight.rearrange("(n t) (q f) -> q t n f", t=BLK, q=QUADS)
    rram_split = rram.rearrange("(n t) (q f) -> q t n f", t=BLK, q=QUADS)

    ctx = ExitStack()
    with ctx:
        def sbuf(name, shape, dt=F32):
            return ctx.enter_context(nc.sbuf_tensor(name, shape, dt))

        def psum(name, shape):
            return ctx.enter_context(nc.psum_tensor(name, shape, F32))

        def sem(name):
            return ctx.enter_context(nc.semaphore(name))

        x_in = sbuf("x_in", [P, 2, GB * NB, FQ])
        x_res = sbuf("x_res", [P, 2, TILES, D])
        xT = sbuf("xT", [P, 2, KD, GT])
        hid = sbuf("hid", [P, 2, KD, GT], F32R)
        x_sum = sbuf("x_sum", [P, GB, KD])
        coef = sbuf("coef", [P, 2, GB, KD])
        q_scale = sbuf("q_scale", [P, B, KD])
        q_emb = sbuf("q_emb", [P, B, KD])
        cond_in = sbuf("cond_in", [BLK, C])
        qT = sbuf("qT", [P, KD, BLK])
        condT = sbuf("condT", [P, KC, BLK])
        b2_col = sbuf("b2_col", [P, KD])
        b3_col = sbuf("b3_col", [P, KD])
        w2_sb = sbuf("w2_sb", [P, KD, D])
        w3_sb = sbuf("w3_sb", [P, KC, D])
        w_in = sbuf("w_in", [P, OB, FQ])
        r_in = sbuf("r_in", [P, OB, FQ])
        w_low = sbuf("w_low", [P, OB, FQ])
        warm = sbuf("warm", [P, D], mybir.dt.bfloat16)
        act_warm = sbuf("act_warm", [1, 1])
        wT = sbuf("wT", [P, KD, D])
        wT_hi = sbuf("wT_hi", [P, KD, D], F32R)
        wT_lo = sbuf("wT_lo", [P, KD, D], F32R)

        hid_ps = [psum(f"hid_ps{m}", [P, GT]) for m in range(KD)]
        out_ps = [psum(f"out_ps{c}", [P, D]) for c in range(TILES)]
        q_ps = out_ps[0][0:BLK]
        LAST_COLS = (slice(0, D // 2), slice(D // 2, D))
        LAST_BANKS = (out_ps[TILES - 1], hid_ps[0])

        def chunk_columns(w, m):
            return w.rearrange("p (c m) -> p m c", m=KD)[:, m]

        s_x_in = [sem(f"x_in_loaded{s}") for s in range(2)]
        s_x_res = [sem(f"x_res_loaded{s}") for s in range(2)]
        s_stored = [sem(f"stored{s}") for s in range(2)]
        s_x_first = sem("first_batch_loaded")
        s_cond_zero = sem("cond_zeroed")
        s_cond = sem("cond_loaded")
        s_b2 = sem("b2_loaded")
        s_b3 = sem("b3_loaded")
        s_w3 = sem("w3_loaded")
        s_w2 = [sem(f"w2_loaded{k}") for k in range(KD)]
        s_w = sem("weight_loaded")
        s_r = sem("rram_loaded")
        s_condT = sem("cond_transposed")
        s_q_ps = sem("q_product_ready")
        s_qT = sem("q_transposed")
        s_q = sem("q_ready")
        s_q_scale = sem("q_scaled")
        s_xT = sem("x_transposed")
        s_sum = sem("x_summed")
        s_coef = sem("coef_ready")
        s_xs = sem("x_scaled")
        s_hid_ps = sem("hidden_product_ready")
        s_hid = sem("hidden_ready")
        s_out_ps = sem("out_product_ready")
        s_out = sem("out_tile_ready")
        s_wstep = sem("weight_step_done")
        s_warm = sem("warm_zeroed")
        s_wT = sem("weight_transposed")
        s_whi = sem("weight_hi_ready")
        s_wlo = sem("weight_lo_ready")

        block = ctx.enter_context(nc.Block())

        @block.sync
        def _(sp):
            def load_x_in(t, s):
                for q in (0, 2, 1, 3):
                    sp.dma_start(x_in[q * BLK:(q + 1) * BLK, s], x_split[2 * t + s, q]).then_inc(s_x_in[s], DMA)

            def load_x_res(t, s):
                sp.dma_start(x_res[:, s], x_tiles[2 * t + s]).then_inc(s_x_res[s], DMA)

            def store(t, s, tiles=TILES):
                for c in range(tiles):
                    sp.wait_ge(s_out, TILES * (2 * t + s) + c + 1)
                    sp.dma_start(out_tiles[2 * t + s, c], x_res[:, s, c]).then_inc(s_stored[s], DMA)

            def reload_x_in(t, s):
                sp.wait_ge(s_xT, GB * (2 * (t - 1) + s + 1))
                load_x_in(t, s)

            def reload_x_res(t, s):
                sp.wait_ge(s_stored[s], DMA * TILES * t)
                load_x_res(t, s)

            sp.dma_start(w3_sb[:], w3_chunks).then_inc(s_w3, DMA)
            for b in range(GB):
                if b == 1:
                    for k in range(KD):
                        sp.dma_start(w2_sb[:, k], w2_chunks[:, k]).then_inc(s_w2[k], DMA)
                for q in (0, 2, 1, 3):
                    sp.dma_start(x_in[q * BLK:(q + 1) * BLK, 0, b * NB:(b + 1) * NB],
                                 x_split[0, q, :, b * NB:(b + 1) * NB]).then_inc(s_x_in[0] if b else s_x_first, DMA)
            load_x_in(0, 1)
            for q in range(QUADS):
                sp.dma_start(w_in[q * BLK:(q + 1) * BLK], weight_split[q]).then_inc(s_w, DMA)
            for q in range(QUADS):
                sp.dma_start(r_in[q * BLK:(q + 1) * BLK], rram_split[q]).then_inc(s_r, DMA)
            load_x_res(0, 0)
            reload_x_in(1, 0)
            load_x_res(0, 1)
            with sp.Fori(0, GROUPS // 2 - 2) as t:
                reload_x_in(t + 1, 1)
                store(t, 0)
                reload_x_res(t + 1, 0)
                reload_x_in(t + 2, 0)
                store(t, 1)
                reload_x_res(t + 1, 1)
            last = GROUPS // 2 - 1
            reload_x_in(last, 1)
            store(last - 1, 0)
            reload_x_res(last, 0)
            store(last - 1, 1)
            reload_x_res(last, 1)
            store(last, 0)
            store(last, 1, TILES - 1)
            for h, cols in enumerate(LAST_COLS):
                sp.wait_ge(s_out, TILES * GROUPS + h)
                sp.dma_start(out_tiles[GROUPS - 1, TILES - 1, :, cols],
                             x_res[:, 1, TILES - 1, cols]).then_inc(s_stored[1], DMA)
            sp.wait_ge(s_stored[0], DMA * TILES * GROUPS // 2)
            sp.wait_ge(s_stored[1], DMA * (TILES * GROUPS // 2 + len(LAST_COLS) - 1))

        @block.gpsimd
        def _(pool):
            pool.dma_start(b3_col[:], b3_chunks).then_inc(s_b3, DMA)
            pool.dma_start(b2_col[:], b2_chunks).then_inc(s_b2, DMA)

        @block.scalar
        def _(act):
            act.wait_ge(s_cond_zero, 1)
            act.dma_start(cond_in[0:B], cond).then_inc(s_cond, DMA)
            act.wait_ge(s_warm, 1)
            nc.scalar.activation(act_warm[:], warm[0:1, 0:1], ACT.Relu)

            act.wait_ge(s_q, 2)
            nc.scalar.mul(q_scale[:], q_emb[:], float(N)).then_inc(s_q_scale, 1)
            act.wait_ge(s_q_scale, 1)

            def scale(t, s):
                for b in range(GB):
                    act.wait_ge(s_coef, GB * (2 * t + s) + b + 1)
                    for k in range(KD):
                        part = xT[:, s, k, b * N:(b + 1) * N]
                        nc.scalar.activation(part, part, ACT.Identity, bias=coef[:, s, b, k:k + 1],
                                             scale=q_scale[:, GB * (2 * t + s) + b, k:k + 1]).then_inc(s_xs, 1)

            scale(0, 0)
            scale(0, 1)
            act.wait_ge(s_wT, 1)
            nc.scalar.copy(wT_hi[:], wT[:]).then_inc(s_whi, 1)
            with act.Fori(0, GROUPS // 2 - 1) as t:
                scale(t + 1, 0)
                scale(t + 1, 1)

        @block.vector
        def _(dve):
            def embed():
                dve.wait_ge(s_q_ps, 1)
                for q in range(QUADS):
                    nc.vector.transpose(qT[q * BLK:(q + 1) * BLK],
                                        q_ps[:, q * FQ:(q + 1) * FQ].rearrange("p (r j) -> p j r", j=KD)
                                        ).then_inc(s_qT, 1)
                dve.wait_ge(s_b3, DMA)
                dve.wait_ge(s_qT, QUADS)
                nc.vector.tensor_tensor(q_emb[:], qT[:, :, 0:B].rearrange("p m b -> p b m"),
                                        b3_col[:].unsqueeze(1).broadcast_to([P, B, KD]), ALU.add).then_inc(s_q, 1)
                dve.wait_ge(s_q, 1)
                nc.vector.tensor_scalar(q_emb[:], q_emb[:], 0.0, None, ALU.max).then_inc(s_q, 1)

            def prepare(t, s, recycled, first=False):
                for b in range(GB):
                    n = GB * (2 * t + s) + b
                    rows = slice(b * NB, (b + 1) * NB)
                    if first and b == 0:
                        dve.wait_ge(s_x_first, DMA * QUADS)
                    else:
                        dve.wait_ge(s_x_in[s], DMA * QUADS * (t + 1))
                    if recycled:
                        dve.wait_ge(s_hid_ps, KD * (2 * (t - 1) + s + 1))
                    nc.vector.transpose(
                        xT[:, s, :, b * N:(b + 1) * N].rearrange("p j (n t) -> p n j t", t=BLK),
                        x_in[:, s, rows].rearrange("p n (r j) -> p n j r", r=BLK)).then_inc(s_xT, 1)
                    dve.wait_ge(s_xT, n + 1)
                    nc.vector.tensor_reduce(x_sum[:, b], xT[:, s, :, b * N:(b + 1) * N],
                                            AX.X, ALU.add).then_inc(s_sum, 1)
                    dve.wait_ge(s_sum, n + 1)
                    if first and b == 0:
                        embed()
                        dve.wait_ge(s_q, 2)
                    nc.vector.tensor_tensor(coef[:, s, b], x_sum[:, b], q_emb[:, n], ALU.mult).then_inc(s_coef, 1)

            def quantize(t, s):
                for m in range(KD):
                    dve.wait_ge(s_hid_ps, KD * (2 * t + s) + m + 1)
                    nc.vector.tensor_scalar(hid[:, s, m], hid_ps[m][:], b2_col[:, m:m + 1], TH_X,
                                            ALU.add, ALU.is_gt).then_inc(s_hid, 1)

            def finish(t, s, tiles=TILES):
                dve.wait_ge(s_x_res[s], DMA * (t + 1))
                for c in range(tiles):
                    dve.wait_ge(s_out_ps, TILES * (2 * t + s) + c + 1)
                    nc.vector.scalar_tensor_tensor(x_res[:, s, c], out_ps[c][:], SC_X, x_res[:, s, c],
                                                   ALU.mult, ALU.add).then_inc(s_out, 1)

            nc.vector.memset(cond_in[:], 0.0).then_inc(s_cond_zero, 1)
            nc.vector.memset(warm[:], 0.0).then_inc(s_warm, 1)
            dve.wait_ge(s_cond, DMA)
            for q in range(QUADS):
                nc.vector.transpose(condT[q * BLK:(q + 1) * BLK],
                                    cond_in[:, q * CQ:(q + 1) * CQ].rearrange("p (r j) -> p j r", j=KC)
                                    ).then_inc(s_condT, 1)
            prepare(0, 0, False, first=True)
            prepare(0, 1, False)
            dve.wait_ge(s_w, QUADS * DMA)
            nc.vector.tensor_scalar(w_low[:], w_in[:], -TH_W, None, ALU.is_lt).then_inc(s_wstep, 1)
            dve.wait_ge(s_wstep, 1)
            nc.vector.scalar_tensor_tensor(w_in[:], w_in[:], TH_W, w_low[:],
                                           ALU.is_gt, ALU.subtract).then_inc(s_wstep, 1)
            dve.wait_ge(s_b2, DMA)
            quantize(0, 0)
            dve.wait_ge(s_r, QUADS * DMA)
            dve.wait_ge(s_wstep, 2)
            nc.vector.scalar_tensor_tensor(w_in[:], w_in[:], SC_W, r_in[:],
                                           ALU.mult, ALU.add).then_inc(s_wstep, 1)
            dve.wait_ge(s_wstep, 3)
            nc.vector.transpose(wT[:].rearrange("p j (n t) -> p n j t", t=BLK),
                                w_in[:].rearrange("p n (r j) -> p n j r", r=BLK)).then_inc(s_wT, 1)
            dve.wait_ge(s_whi, 1)
            nc.vector.tensor_tensor(wT_lo[:], wT[:], wT_hi[:].bitcast(F32), ALU.subtract).then_inc(s_wlo, 1)
            with dve.Fori(0, GROUPS // 2 - 1) as t:
                prepare(t + 1, 0, True)
                quantize(t, 1)
                finish(t, 0)
                prepare(t + 1, 1, True)
                quantize(t + 1, 0)
                finish(t, 1)
            last = GROUPS // 2 - 1
            quantize(last, 1)
            finish(last, 0)
            finish(last, 1, TILES - 1)
            for h, cols in enumerate(LAST_COLS):
                dve.wait_ge(s_out_ps, TILES * GROUPS + h)
                nc.vector.scalar_tensor_tensor(x_res[:, 1, TILES - 1, cols], LAST_BANKS[h][:, cols], SC_X,
                                               x_res[:, 1, TILES - 1, cols], ALU.mult, ALU.add).then_inc(s_out, 1)

        @block.tensor
        def _(pe):
            pe.wait_ge(s_warm, 1)
            for _ in range(WARM):
                nc.tensor.matmul(out_ps[TILES - 1][:], warm[:, 0:P], warm[:], start=True, stop=True)
            pe.wait_ge(s_condT, QUADS)
            pe.wait_ge(s_w3, DMA)
            for k in range(KC):
                mm = nc.tensor.matmul(q_ps, condT[:, k], w3_sb[:, k], start=(k == 0), stop=(k == KC - 1))
            mm.then_inc(s_q_ps, 1)
            for _ in range(WARM_2):
                nc.tensor.matmul(out_ps[TILES - 1][:], warm[:, 0:P], warm[:], start=True, stop=True)

            def hidden(t, s):
                pe.wait_ge(s_xs, GB * KD * (2 * t + s + 1))
                for m in range(KD):
                    pe.wait_ge(s_hid, KD * (2 * t + s - 1) + m + 1)
                    for k in range(KD):
                        mm = nc.tensor.matmul(hid_ps[m][:], chunk_columns(w2_sb[:, k], m), xT[:, s, k],
                                              start=(k == 0), stop=(k == KD - 1))
                    mm.then_inc(s_hid_ps, 1)

            def project_tile(s, c, bank, cols=slice(0, D)):
                for k in range(KD):
                    for w in (wT_lo, wT_hi):
                        mm = nc.tensor.matmul(bank[:, cols], hid[:, s, k, c * P:(c + 1) * P], w[:, k, cols],
                                              start=(k == 0 and w is wT_lo), stop=(k == KD - 1 and w is wT_hi))
                mm.then_inc(s_out_ps, 1)

            def project(t, s, first, tiles=TILES):
                pe.wait_ge(s_hid, KD * (2 * t + s + 1))
                for c in range(tiles):
                    if not first:
                        pe.wait_ge(s_out, TILES * (2 * t + s - 1) + c + 1)
                    project_tile(s, c, out_ps[c])

            for k in range(KD):
                pe.wait_ge(s_w2[k], DMA)
                pe.wait_ge(s_xs, k + 1)
                for m in range(KD):
                    nc.tensor.matmul(hid_ps[m][:, 0:N], chunk_columns(w2_sb[:, k], m), xT[:, 0, k, 0:N],
                                     start=(k == 0), stop=(k == KD - 1))
            pe.wait_ge(s_xs, 2 * KD)
            for m in range(KD):
                for k in range(KD):
                    mm = nc.tensor.matmul(hid_ps[m][:, N:GT], chunk_columns(w2_sb[:, k], m), xT[:, 0, k, N:GT],
                                          start=(k == 0), stop=(k == KD - 1))
                mm.then_inc(s_hid_ps, 1)

            hidden(0, 1)
            pe.wait_ge(s_wlo, 1)
            project(0, 0, True)
            with pe.Fori(0, GROUPS // 2 - 1) as t:
                hidden(t + 1, 0)
                project(t, 1, False)
                hidden(t + 1, 1)
                project(t + 1, 0, False)
            project(GROUPS // 2 - 1, 1, False, TILES - 1)
            pe.wait_ge(s_out, TILES * (GROUPS - 1))
            for bank, cols in zip(LAST_BANKS, LAST_COLS):
                project_tile(1, TILES - 1, bank, cols)


_INS = ["x", "cond_1024", "L0_cond_W3", "L0_cond_b3", "L0_cond_W2", "L0_cond_b2", "L0_ffn_weight",
        "L0_ffn_rram_variation"]


def kernel(**inputs):
    import numpy as np
    import concourse.bacc as bacc
    from concourse import mybir as mb
    from concourse.bass_utils import run_bass_kernel_spmd

    nc = bacc.Bacc("TRN2", target_bir_lowering=False, num_devices=1)
    arrays, args = {}, []
    for name in _INS:
        a = np.ascontiguousarray(inputs[name])
        arrays[f"in_{name}"] = a
        args.append(nc.dram_tensor(f"in_{name}", a.shape, mb.dt.from_np(a.dtype), kind="ExternalInput").ap())
    shape = inputs["x"].shape
    args.append(nc.dram_tensor("out", shape, mb.dt.float32, kind="ExternalOutput").ap())
    adaln_ffn_kernel(nc, *args)
    r = run_bass_kernel_spmd(nc, [arrays], core_ids=[0])
    return r.results[0]["out"]
```
